# Optimizing a Trainium2 kernel written in Bass

```python
import numpy as np
import jax
import jax.numpy as jnp

def _softmax(x, axis=-1):
    return jax.nn.softmax(x, axis=axis)

def _gelu(x):
    return jax.nn.gelu(x, approximate=True)

def _silu(x):
    return jax.nn.silu(x)

def _sigmoid(x):
    return jax.nn.sigmoid(x)

def _layernorm(x, axis=-1, eps=1e-05):
    m = jnp.mean(x, axis=axis, keepdims=True)
    v = jnp.var(x, axis=axis, keepdims=True)
    return (x - m) / jnp.sqrt(v + eps)

def _scatter_add(tgt, idx, src, axis=0):
    return tgt.at[idx].add(src)

def _segment_sum(src, seg, n):
    return jax.ops.segment_sum(src, seg, n)
kernel_name = 'mk_sandwich_d1_jaxref_r4_0d2776'

def setup_inputs(seed: int=0):
    np.random.seed(seed)
    _w = jnp.asarray

    def _L0_attn_setup():
        import jax, jax.numpy as jnp
        import numpy as np
        EMBED = 1024
        HEADS = 16
        HEAD_DIM = EMBED // HEADS
        ROT = 64
        B, S = (1, 512)
        MASK_VAL = -1000000000.0

        def _rotate_every_two(x):
            r = jnp.stack((x[..., 1::2], x[..., ::2]), axis=-1)
            return r.reshape(x.shape)

        def _fixed_pos_embedding(seq_len, rot_dim):
            inv_freq = 1.0 / 10000.0 ** (jnp.arange(0, rot_dim, 2, dtype=jnp.float32) / rot_dim)
            t = jnp.arange(seq_len, dtype=jnp.float32)
            sinusoid = jnp.einsum('i,j->ij', t, inv_freq)
            return (jnp.sin(sinusoid), jnp.cos(sinusoid))

        def _apply_rotary(x, sin, cos):
            sin = jnp.repeat(sin[None, :, None, :], 2, axis=3)
            cos = jnp.repeat(cos[None, :, None, :], 2, axis=3)
            return x * cos + _rotate_every_two(x) * sin
        key = jax.random.key(seed)
        ks = jax.random.split(key, 5)
        sc = 0.02
        return {'hidden_states': jax.random.normal(ks[0], (B, S, EMBED), jnp.float32), 'Wq': jax.random.normal(ks[1], (EMBED, EMBED), jnp.float32) * sc, 'Wk': jax.random.normal(ks[2], (EMBED, EMBED), jnp.float32) * sc, 'Wv': jax.random.normal(ks[3], (EMBED, EMBED), jnp.float32) * sc, 'Wo': jax.random.normal(ks[4], (EMBED, EMBED), jnp.float32) * sc}
    _L0_attn_in = _L0_attn_setup()

    def _L0_ffn_setup():
        import jax, jax.numpy as jnp
        import numpy as np
        NF4 = jnp.array([-1.0, -0.6961928009986877, -0.5250730514526367, -0.39491748809814453, -0.28444138169288635, -0.18477343022823334, -0.09105003625154495, 0.0, 0.07958029955625534, 0.16093020141124725, 0.24611230194568634, 0.33791524171829224, 0.44070982933044434, 0.5626170039176941, 0.7229568362236023, 1.0], dtype=jnp.float32)
        BLOCK = 64

        def dequant_nf4(codes, scales):
            out_dim, in_dim = codes.shape
            vals = NF4[codes].reshape(out_dim, in_dim // BLOCK, BLOCK)
            return (vals * scales[:, :, None]).reshape(out_dim, in_dim)
        key = jax.random.key(seed)
        ks = jax.random.split(key, 7)
        H, I = (1024, 2752)
        B, S = (4, 512)
        return {'x': jax.random.normal(ks[0], (B, S, H), dtype=jnp.float32), 'gate_codes': jax.random.randint(ks[1], (I, H), 0, 16, dtype=jnp.int32), 'gate_scales': jax.random.uniform(ks[2], (I, H // BLOCK), dtype=jnp.float32) * 0.02, 'up_codes': jax.random.randint(ks[3], (I, H), 0, 16, dtype=jnp.int32), 'up_scales': jax.random.uniform(ks[4], (I, H // BLOCK), dtype=jnp.float32) * 0.02, 'down_codes': jax.random.randint(ks[5], (H, I), 0, 16, dtype=jnp.int32), 'down_scales': jax.random.uniform(ks[6], (H, I // BLOCK), dtype=jnp.float32) * 0.02}
    _L0_ffn_in = _L0_ffn_setup()
    _d = {'L0_attn_hidden_states': _L0_attn_in['hidden_states'], 'L0_attn_Wq': _L0_attn_in['Wq'], 'L0_attn_Wk': _L0_attn_in['Wk'], 'L0_attn_Wv': _L0_attn_in['Wv'], 'L0_attn_Wo': _L0_attn_in['Wo'], 'L0_ffn_gate_codes': _L0_ffn_in['gate_codes'], 'L0_ffn_gate_scales': _L0_ffn_in['gate_scales'], 'L0_ffn_up_codes': _L0_ffn_in['up_codes'], 'L0_ffn_up_scales': _L0_ffn_in['up_scales'], 'L0_ffn_down_codes': _L0_ffn_in['down_codes'], 'L0_ffn_down_scales': _L0_ffn_in['down_scales']}
    _x0 = _d['L0_attn_hidden_states']
    _d['L0_attn_hidden_states'] = jax.random.normal(jax.random.fold_in(jax.random.key(seed), 1), (1, 2048, 1024), dtype=_x0.dtype)
    del _x0
    return _d

def reference(L0_attn_hidden_states, L0_attn_Wq, L0_attn_Wk, L0_attn_Wv, L0_attn_Wo, L0_ffn_gate_codes, L0_ffn_gate_scales, L0_ffn_up_codes, L0_ffn_up_scales, L0_ffn_down_codes, L0_ffn_down_scales):

    def _L0_attn_ref(hidden_states, Wq, Wk, Wv, Wo):
        import jax, jax.numpy as jnp
        import numpy as np
        EMBED = 1024
        HEADS = 16
        HEAD_DIM = EMBED // HEADS
        ROT = 64
        B, S = (1, 512)
        MASK_VAL = -1000000000.0

        def _rotate_every_two(x):
            r = jnp.stack((x[..., 1::2], x[..., ::2]), axis=-1)
            return r.reshape(x.shape)

        def _fixed_pos_embedding(seq_len, rot_dim):
            inv_freq = 1.0 / 10000.0 ** (jnp.arange(0, rot_dim, 2, dtype=jnp.float32) / rot_dim)
            t = jnp.arange(seq_len, dtype=jnp.float32)
            sinusoid = jnp.einsum('i,j->ij', t, inv_freq)
            return (jnp.sin(sinusoid), jnp.cos(sinusoid))

        def _apply_rotary(x, sin, cos):
            sin = jnp.repeat(sin[None, :, None, :], 2, axis=3)
            cos = jnp.repeat(cos[None, :, None, :], 2, axis=3)
            return x * cos + _rotate_every_two(x) * sin
        b, s, e = hidden_states.shape
        q = (hidden_states @ Wq).reshape(b, s, HEADS, HEAD_DIM)
        k = (hidden_states @ Wk).reshape(b, s, HEADS, HEAD_DIM)
        v = (hidden_states @ Wv).reshape(b, s, HEADS, HEAD_DIM)
        sin, cos = _fixed_pos_embedding(s, ROT)
        q = jnp.concatenate([_apply_rotary(q[..., :ROT], sin, cos), q[..., ROT:]], axis=-1)
        k = jnp.concatenate([_apply_rotary(k[..., :ROT], sin, cos), k[..., ROT:]], axis=-1)
        q = q.transpose(0, 2, 1, 3)
        k = k.transpose(0, 2, 1, 3)
        v = v.transpose(0, 2, 1, 3)
        logits = jnp.einsum('bhqd,bhkd->bhqk', q, k)
        causal = jnp.tril(jnp.ones((s, s), dtype=bool))[None, None]
        logits = jnp.where(causal, logits, MASK_VAL)
        logits = logits / jnp.sqrt(jnp.float32(HEAD_DIM))
        attn = jax.nn.softmax(logits, axis=-1)
        out = jnp.einsum('bhqk,bhkd->bhqd', attn, v)
        out = out.transpose(0, 2, 1, 3).reshape(b, s, e)
        return out @ Wo

    def _L0_ffn_ref(x, gate_codes, gate_scales, up_codes, up_scales, down_codes, down_scales):
        import jax, jax.numpy as jnp
        import numpy as np
        NF4 = jnp.array([-1.0, -0.6961928009986877, -0.5250730514526367, -0.39491748809814453, -0.28444138169288635, -0.18477343022823334, -0.09105003625154495, 0.0, 0.07958029955625534, 0.16093020141124725, 0.24611230194568634, 0.33791524171829224, 0.44070982933044434, 0.5626170039176941, 0.7229568362236023, 1.0], dtype=jnp.float32)
        BLOCK = 64

        def dequant_nf4(codes, scales):
            out_dim, in_dim = codes.shape
            vals = NF4[codes].reshape(out_dim, in_dim // BLOCK, BLOCK)
            return (vals * scales[:, :, None]).reshape(out_dim, in_dim)
        Wg = dequant_nf4(gate_codes, gate_scales)
        Wu = dequant_nf4(up_codes, up_scales)
        Wd = dequant_nf4(down_codes, down_scales)
        gate = jnp.einsum('bsh,ih->bsi', x, Wg)
        up = jnp.einsum('bsh,ih->bsi', x, Wu)
        inter = jax.nn.silu(gate) * up
        return jnp.einsum('bsi,hi->bsh', inter, Wd)
    x = L0_attn_hidden_states
    x = x + _layernorm(_L0_attn_ref(_layernorm(x, axis=-1), L0_attn_Wq, L0_attn_Wk, L0_attn_Wv, L0_attn_Wo), axis=-1)
    x = x + _layernorm(_L0_ffn_ref(_layernorm(x, axis=-1), L0_ffn_gate_codes, L0_ffn_gate_scales, L0_ffn_up_codes, L0_ffn_up_scales, L0_ffn_down_codes, L0_ffn_down_scales), axis=-1)
    return x

_drawn_inputs = setup_inputs


def setup_inputs(seed=0):
    import zlib

    import numpy as np

    out = dict(_drawn_inputs(seed))
    spreads = {}
    factors = {}
    for name, (base, spread) in spreads.items():
        noise = np.random.default_rng([zlib.crc32(name.encode()), seed]).standard_normal(out[name].shape)
        drawn = base * np.exp(spread * noise) if base else spread * noise
        out[name] = jnp.asarray(drawn.astype(out[name].dtype))
    for name, factor in factors.items():
        out[name] = (out[name] * factor).astype(out[name].dtype)
    return out
```

```python
from contextlib import ExitStack

import numpy as np

import concourse.bass as bass
from concourse import mybir
from concourse.alu_op_type import AluOpType as ALU

F32 = mybir.dt.float32
F16 = mybir.dt.float16
BF16 = mybir.dt.bfloat16
I32 = mybir.dt.int32
U32 = mybir.dt.uint32
ACT = mybir.ActivationFunctionType
AX_X = mybir.AxisListType.X

P = 128
S = 2048
E = 1024
HEADS = 16
D = E // HEADS
HALF = D // 2
I = 2752
BLOCK = 64
ST = S // P
KT = E // P
CH = 512
SC = S // CH
GW = 2 * P
NG = -(-I // GW)
IP = NG * GW
UNITS = KT * GW // CH
EPS = 1e-5

H_SCALE = 2.0 ** 10
W_SCALE = 2.0 ** 14
QKV_DOWN = 2.0 ** -20
P_SCALE = 2.0 ** 15
MASKED = -(2.0 ** 100)

NF4 = [-1.0, -0.6961928009986877, -0.5250730514526367, -0.39491748809814453, -0.28444138169288635,
       -0.18477343022823334, -0.09105003625154495, 0.0, 0.07958029955625534, 0.16093020141124725,
       0.24611230194568634, 0.33791524171829224, 0.44070982933044434, 0.5626170039176941,
       0.7229568362236023, 1.0]
ZERO_CODE = 7


def nf4_line(i, j):
    a, b = np.float32(NF4[i]), np.float32(NF4[j])
    slope = np.float32(np.float64(b) - np.float64(a)) if j > i else np.float32(0.31)
    for k in sorted(range(-60, 61), key=abs):
        d = np.float32(slope + np.float32(k) * np.spacing(slope))
        e0 = np.float32(np.float64(a) - (i - ZERO_CODE) * np.float64(d))
        for m in sorted(range(-8, 9), key=abs):
            e = np.float32(e0 + np.float32(m) * np.spacing(e0))
            if all(np.float32(np.float64(c - ZERO_CODE) * np.float64(d) + np.float64(e)) == v
                   for c, v in ((i, a), (j, b))):
                return float(d), float(e)
    raise ValueError("no such line")


BELOW = [nf4_line(0, 0), nf4_line(1, 2), nf4_line(3, 4), nf4_line(5, 6)]
ABOVE = [nf4_line(8, 9), nf4_line(10, 11), nf4_line(12, 13), nf4_line(14, 15)]


class Signal:

    def __init__(self, sem, credit=0):
        self.sem, self.credit = sem, credit

    def give(self, eng):
        eng.sem_inc(self.sem, self.credit)

    def done(self, eng, item):
        eng.wait_ge(self.sem, item + 1 + self.credit)

    def room(self, eng, item):
        eng.wait_ge(self.sem, item + 1)


class Loads:

    def __init__(self, sems, n=1):
        self.sems, self.n = sems, n

    def done(self, eng, slot, use):
        eng.wait_ge(self.sems[slot], (use + 1) * (16 * self.n))


class Step:

    def __init__(self, u, turn=None):
        self.u, self.turn = u, turn

    def has(self, k, n):
        return self.turn is not None or 0 <= self.u + k < n

    def item(self, k):
        return self.u + k if self.turn is None else self.turn * 2 + (self.u + k)

    def use(self, k):
        return (self.u + k) // 2 if self.turn is None else self.turn + (self.u + k) // 2

    def slot(self, k):
        return (self.u + k) % 2


def pipeline(eng, step, before, after, n):
    lo = after + after % 2
    hi = n - before - before % 2
    for s in range(-before, lo):
        step(Step(s))
    with eng.Fori(0, (hi - lo) // 2) as turn:
        for u in range(2):
            step(Step(lo + u, turn))
    for s in range(hi, n + after):
        step(Step(s))


class Chain:

    def __init__(self, eng, sem, base=0):
        self.eng, self.sem, self.at = eng, sem, base

    def link(self, ins):
        ins.then_inc(self.sem, 1)
        self.at = self.at + 1

    def wait(self):
        self.eng.wait_ge(self.sem, self.at)

    def stop(self):
        self.wait()
        self.eng.sem_inc(self.sem, 1)
        self.at = self.at + 1


def build(nc, x, wq, wk, wv, wo, cos, sin, codes, scales, scales_flat, out):
    ctx = ExitStack()
    with ctx:
        def sb(name, shape, dt, c=ctx):
            return c.enter_context(nc.sbuf_tensor(name, shape, dt))

        def ps(name, shape, dt, c):
            return c.enter_context(nc.psum_tensor(name, shape, dt))

        def sem(name):
            return ctx.enter_context(nc.semaphore(name))

        def signal(name, credit=0):
            return Signal(sem(name), credit)

        def loads(name, slots=1, n=1):
            return Loads([sem(f"{name}{i}") for i in range(slots)], n)

        qk_dram = nc.dram_tensor("qk_pairs", (2, HEADS, 2, D, S), F16, kind="Internal").ap()
        x1_dram = nc.dram_tensor("x1_rows", (S, E), F32, kind="Internal").ap()

        region1 = sb("region1", [P, 2 * KT * S], F16)
        region2 = sb("region2", [P, 2 * KT * S], F16)
        hT = region1[:, :].rearrange("p (a k s) -> p a k s", a=2, k=KT)
        o_rows = region1[:, :].bitcast(F32).rearrange("p (t e) -> p t e", t=ST)
        y_rows = region1[:, :].bitcast(F32).rearrange("p (t e) -> p t e", t=ST)
        wv_f32 = region2[:, 0:2 * KT * E].bitcast(F32).rearrange("p (k n) -> p k n", k=KT)
        v_rows = region2[:, :].rearrange("p (t h c) -> p t h c", t=ST, h=HEADS)
        xnT = region2[:, :].rearrange("p (a k s) -> p a k s", a=2, k=KT)

        absmax = sb("absmax", [P, 8], F32)
        allmax = sb("allmax", [P, 8], F32)
        p2 = sb("p2", [P, 8], F32)
        wfac = sb("wfac", [P, 8], F32)
        coef = sb("coef", [P, 8], F32)
        minus_half = sb("minus_half", [P, 1], F32)
        eps = sb("eps", [P, 1], F32)
        c04 = ctx.enter_context(ExitStack())
        ident = sb("ident", [P, P], F32, c04)
        ident_bf = sb("ident_bf", [P, P], BF16, c04)
        mask_f32 = sb("mask_f32", [P, P], F32, c04)
        mask_bf = sb("mask_bf", [P, P], BF16, c04)
        sums = sb("sums", [P, ST, HEADS, SC], F32, c04)
        Q_, K_, O_, V_, G_, U_, D_ = range(7)

        def col(t, n):
            return t[:, n:n + 1]

        def powers(v, chain, a, b):
            chain.link(v.tensor_scalar(p2[:, a:b], allmax[:, a:b], 2.0 ** -60, 2.0 ** 60, ALU.max, ALU.min))
            chain.wait()
            chain.link(v.tensor_single_scalar(p2[:, a:b].bitcast(U32), p2[:, a:b].bitcast(U32), 0x7F800000,
                                              ALU.bitwise_and))
            chain.wait()
            chain.link(v.reciprocal(wfac[:, a:b], p2[:, a:b]))
            chain.wait()
            chain.link(v.tensor_scalar(wfac[:, a:b], wfac[:, a:b], W_SCALE, None, ALU.mult))
            chain.wait()

        def product(v, chain, n, cols, factor):
            chain.link(v.tensor_scalar(col(coef, n), col(p2, cols[0]), factor, None, ALU.mult))
            for c in cols[1:]:
                chain.wait()
                chain.link(v.tensor_scalar(col(coef, n), col(coef, n), col(p2, c), None, ALU.mult))

        c01 = ctx.enter_context(ExitStack())
        wv_pair = sb("wv_pair", [P, 2, KT, E], F16, c01)
        c0 = ctx.enter_context(ExitStack())
        flat = sb("flat", [P, 3, I * E // BLOCK // P], F32, c0)
        vmax = sb("vmax", [P, KT], F32, c0)
        d_wv = loads("d_wv", KT)
        d_flat = loads("d_flat", 1, 3)
        s_c0 = sem("s_c0")
        s_max0 = signal("s_max0")
        s_all0 = signal("s_all0")
        s_id = signal("s_id")
        s_fac0 = signal("s_fac0")
        s_wvhi = signal("s_wvhi")
        with nc.Block() as block:
            @block.sync
            def _(sp):
                wv_v = wv.rearrange("(k p) n -> p k n", p=P)
                for m in range(3):
                    sp.dma_start(flat[:, m, :], scales_flat[m]).then_inc(d_flat.sems[0], 16)
                for k in range(KT):
                    sp.dma_start(wv_f32[:, k, :], wv_v[:, k, :]).then_inc(d_wv.sems[k], 16)

            @block.gpsimd
            def _(pool):
                pool.memset(ident[:, :], 0.0).then_inc(s_id.sem, 1)
                pool.memset(mask_f32[:, :], 0.0).then_inc(s_id.sem, 1)
                pool.memset(minus_half[:, :], -0.5).then_inc(s_id.sem, 1)
                pool.memset(eps[:, :], EPS).then_inc(s_id.sem, 1)
                s_id.done(pool, 3)
                pool.affine_select(out=ident[:, :], in_=ident[:, :], compare_op=ALU.not_equal, fill=1.0,
                                   base=0, pattern=[[-1, P]], channel_multiplier=1).then_inc(s_id.sem, 1)
                pool.affine_select(out=mask_f32[:, :], in_=mask_f32[:, :], compare_op=ALU.is_ge, fill=MASKED,
                                   base=0, pattern=[[-1, P]], channel_multiplier=1).then_inc(s_id.sem, 1)
                s_max0.done(pool, 0)
                pool.partition_all_reduce(allmax[:, V_:D_ + 1], absmax[:, V_:D_ + 1], P,
                                          bass.bass_isa.ReduceOp.max).then_inc(s_all0.sem, 1)

            @block.vector
            def _(v):
                chain = Chain(v, s_c0)
                chain.link(v.memset(sums[:, :, :, :], 0.0))
                s_id.done(v, 5)
                chain.link(v.tensor_copy(ident_bf[:, :], ident[:, :]))
                chain.link(v.tensor_copy(mask_bf[:, :], mask_f32[:, :]))
                d_flat.done(v, 0, 0)
                for m, c in enumerate((G_, U_, D_)):
                    chain.link(v.tensor_reduce(col(absmax, c), flat[:, m, :], AX_X, ALU.max,
                                               apply_absolute_value=True))
                for k in range(KT):
                    d_wv.done(v, k, 0)
                    chain.link(v.tensor_reduce(col(vmax, k), wv_f32[:, k, :], AX_X, ALU.max,
                                               apply_absolute_value=True))
                chain.wait()
                v.tensor_reduce(col(absmax, V_), vmax[:, :], AX_X, ALU.max).then_inc(s_max0.sem, 1)
                s_all0.done(v, 0)
                powers(v, chain, V_, D_ + 1)
                product(v, chain, 2, [G_], 2.0 ** -24)
                product(v, chain, 4, [G_, U_, D_], 2.0 ** -7)
                chain.wait()
                v.tensor_scalar(col(coef, 3), col(wfac, G_), 2.0 ** -45, None,
                                ALU.mult).then_inc(s_fac0.sem, 1)
                for k in range(KT):
                    s_wvhi.done(v, k)
                    v.scalar_tensor_tensor(out=wv_pair[:, 1, k, :], in0=wv_f32[:, k, :], scalar=col(wfac, V_),
                                           in1=wv_pair[:, 0, k, :], op0=ALU.mult, op1=ALU.subtract)

            @block.scalar
            def _(a):
                s_fac0.done(a, 0)
                for k in range(KT):
                    a.activation(wv_pair[:, 0, k, :], wv_f32[:, k, :], ACT.Copy,
                                 scale=col(wfac, V_)).then_inc(s_wvhi.sem, 1)
        c0.close()

        def layernorm_stats(v, chain, parts, st, variance):
            for n, part in enumerate(parts):
                chain.link(v.bn_stats(st[:, 6 * n:6 * n + 6], part))
            chain.stop()
            v.bn_aggr(st[:, 12:14], st[:, 0:12]).then_inc(variance.sem, 1)

        def inverse_root(pool, st, own, root, i):
            pool.tensor_tensor(st[:, 13:14], st[:, 13:14], eps[:, :], ALU.add).then_inc(own.sem, 1)
            own.done(pool, i)
            pool.tensor_tensor(st[:, 14:15], st[:, 13:14], minus_half[:, :], ALU.pow).then_inc(root.sem, 1)

        c1 = ctx.enter_context(ExitStack())
        xt = sb("xt", [P, 2, E], F32, c1)
        ht = sb("ht", [P, 2, E], F32, c1)
        wst = sb("wst", [P, 2, 3, CH], F32, c1)
        wmax = sb("wmax", [P, 3, ST], F32, c1)
        st1 = sb("st1", [P, 2, 16], F32, c1)
        tp = ps("tp1", [P, 2, KT, P], F32, c1)
        vp = ps("vp", [P, 2, 2, CH], F32, c1)
        d_x = loads("d_x", 2)
        d_ws = loads("d_ws", 2, 3)
        s_c1 = sem("s_c1")
        s_h = signal("s_h", 2)
        s_wm = signal("s_wm", 2)
        s_T1 = signal("s_T1", 2)
        s_thi = signal("s_thi")
        s_tlo = signal("s_tlo", 2)
        s_V = signal("s_V")
        s_vhi = signal("s_vhi")
        s_vlo = signal("s_vlo", 2)
        s_var1 = signal("s_var1")
        s_eps1 = signal("s_eps1")
        s_root1 = signal("s_root1")
        s_fac1 = signal("s_fac1")
        s_all1 = signal("s_all1")
        CHAIN1 = 4

        with nc.Block() as block:
            w_parts = [w.rearrange("r (b n) -> (r b) n", n=CH).rearrange("(i p) n -> i p n", p=P)
                       for w in (wq.rearrange("t p n -> (t p) n"), wk.rearrange("t p n -> (t p) n"), wo)]
            x_tiles = x.rearrange("(t p) e -> t p e", p=P)

            @block.sync
            def _(sp):
                def step(i, it, u):
                    s_h.room(sp, i)
                    sp.dma_start(xt[:, u, :], x_tiles[bass.ds(i, 1)].rearrange("a p e -> p (a e)")
                                 ).then_inc(d_x.sems[u], 16)
                    s_wm.room(sp, i)
                    for m in range(3):
                        sp.dma_start(wst[:, u, m, :], w_parts[m][bass.ds(i, 1)].rearrange("a p e -> p (a e)")
                                     ).then_inc(d_ws.sems[u], 16)
                with sp.Fori(0, ST // 2) as it:
                    for u in range(2):
                        step(it * 2 + u, it, u)

            @block.tensor
            def _(pe):
                s_T1.give(pe)

                def transposes(i, u):
                    s_h.done(pe, i)
                    s_tlo.room(pe, i)
                    for k in range(KT):
                        mm = pe.transpose(tp[:, u, k, :], ht[:, u, k * P:(k + 1) * P], ident[:, :])
                    mm.then_inc(s_T1.sem, 1)

                def project(i, u):
                    s_tlo.done(pe, i)
                    s_vlo.room(pe, i)
                    for n in range(2):
                        for k in range(KT):
                            for a, b in ((0, 0), (0, 1), (1, 0)):
                                mm = pe.matmul(vp[:, u, n, :], hT[:, a, k, bass.ds(i * P, P)],
                                               wv_pair[:, b, k, n * CH:(n + 1) * CH],
                                               start=(k == 0 and a == b), stop=(k == KT - 1 and a == 1))
                    mm.then_inc(s_V.sem, 1)

                transposes(0, 0)
                with pe.Fori(0, ST // 2 - 1) as it:
                    for u in range(2):
                        transposes(it * 2 + u + 1, 1 - u)
                        project(it * 2 + u, u)
                transposes(ST - 1, 1)
                project(ST - 2, 0)
                project(ST - 1, 1)

            @block.scalar
            def _(a):
                def hi(i, u):
                    s_T1.done(a, i)
                    a.activation(hT[:, 0, :, bass.ds(i * P, P)], tp[:, u, :, :], ACT.Copy).then_inc(s_thi.sem, 1)

                def v_hi(i, u):
                    s_V.done(a, i)
                    a.activation(v_rows[:, bass.ds(i, 1), :, 0:D].rearrange("p a h d -> p (a h) d"),
                                 vp[:, u, :, :].rearrange("p n (h d) -> p (n h) d", d=D), ACT.Copy,
                                 scale=QKV_DOWN).then_inc(s_vhi.sem, 1)

                hi(0, 0)
                with a.Fori(0, ST // 2 - 1) as it:
                    for u in range(2):
                        hi(it * 2 + u + 1, 1 - u)
                        v_hi(it * 2 + u, u)
                hi(ST - 1, 1)
                v_hi(ST - 2, 0)
                v_hi(ST - 1, 1)

            @block.vector
            def _(v):
                for s in (s_h, s_wm, s_tlo, s_vlo):
                    s.give(v)

                def rows(i, it, u):
                    chain = Chain(v, s_c1, i * CHAIN1)
                    d_x.done(v, u, it)
                    layernorm_stats(v, chain, (xt[:, u, 0:CH], xt[:, u, CH:E]), st1[:, u, :], s_var1)
                    d_ws.done(v, u, it)
                    for m in range(3):
                        mx = v.tensor_reduce(wmax[:, m, bass.ds(i, 1)], wst[:, u, m, :], AX_X, ALU.max,
                                             apply_absolute_value=True)
                    mx.then_inc(s_wm.sem, 1)
                    s_root1.done(v, i)
                    chain.link(v.tensor_scalar(st1[:, u, 14:15], st1[:, u, 14:15], H_SCALE, None, ALU.mult))
                    chain.wait()
                    s_T1.room(v, i)
                    v.tensor_scalar(ht[:, u, :], xt[:, u, :], st1[:, u, 12:13], st1[:, u, 14:15],
                                    ALU.subtract, ALU.mult).then_inc(s_h.sem, 1)

                def lo(i, u):
                    s_thi.done(v, i)
                    v.tensor_tensor(hT[:, 1, :, bass.ds(i * P, P)], tp[:, u, :, :],
                                    hT[:, 0, :, bass.ds(i * P, P)], ALU.subtract).then_inc(s_tlo.sem, 1)

                def v_lo(i, u):
                    s_vhi.done(v, i)
                    v.scalar_tensor_tensor(
                        out=v_rows[:, bass.ds(i, 1), :, D:2 * D].rearrange("p a h d -> p (a h) d"),
                        in0=vp[:, u, :, :].rearrange("p n (h d) -> p (n h) d", d=D), scalar=QKV_DOWN,
                        in1=v_rows[:, bass.ds(i, 1), :, 0:D].rearrange("p a h d -> p (a h) d"),
                        op0=ALU.mult, op1=ALU.subtract).then_inc(s_vlo.sem, 1)

                rows(0, 0, 0)
                rows(1, 0, 1)
                lo(0, 0)
                with v.Fori(0, ST // 2 - 1) as it:
                    for u in range(2):
                        rows(it * 2 + u + 2, it + 1, u)
                        lo(it * 2 + u + 1, 1 - u)
                        v_lo(it * 2 + u, u)
                lo(ST - 1, 1)
                v_lo(ST - 2, 0)
                v_lo(ST - 1, 1)
                chain = Chain(v, s_c1, ST * CHAIN1)
                s_wm.done(v, ST - 1)
                v.tensor_reduce(absmax[:, 0:3], wmax[:, :, :], AX_X, ALU.max).then_inc(s_fac1.sem, 1)
                s_all1.done(v, 0)
                powers(v, chain, Q_, O_ + 1)
                product(v, chain, 0, [Q_, K_], 2.0 ** -11)
                product(v, chain, 1, [V_, O_], 2.0 ** -18)
                chain.wait()

            @block.gpsimd
            def _(pool):
                with pool.Fori(0, ST // 2) as it:
                    for u in range(2):
                        s_var1.done(pool, it * 2 + u)
                        inverse_root(pool, st1[:, u, :], s_eps1, s_root1, it * 2 + u)
                s_fac1.done(pool, 0)
                pool.partition_all_reduce(allmax[:, 0:3], absmax[:, 0:3], P,
                                          bass.bass_isa.ReduceOp.max).then_inc(s_all1.sem, 1)
        c1.close()
        c01.close()

        c2 = ctx.enter_context(ExitStack())
        cos_sb = sb("cos_sb", [P, S], F32, c2)
        sin_sb = sb("sin_sb", [P, S], F32, c2)
        wt = sb("wt", [P, 2, KT, P], F32, c2)
        wt_pair = sb("wt_pair", [P, 2, 2, KT, P], F16, c2)
        swap = sb("swap", [P, 2, CH], F32, c2)
        rot = sb("rot", [P, 2, 2, CH], F32, c2)
        r_pair = sb("r_pair", [P, 2, 2, S], F16, c2)
        pq = ps("pq", [P, SC, CH], F32, c2)
        d_tab = loads("d_tab", 1, 2)
        d_wt = loads("d_wt", 2)
        d_qk = loads("d_qk", 2, 8)
        s_wthi = signal("s_wthi")
        s_wtlo = signal("s_wtlo", 2)
        s_pq = signal("s_pq", 2 * SC)
        s_sw = signal("s_sw")
        s_t1 = signal("s_t1", SC)
        s_t2 = signal("s_t2", 2)
        s_r = signal("s_r")
        s_rhi = signal("s_rhi", 2)
        s_rlo = signal("s_rlo", 2)
        JT = 2 * KT
        with nc.Block() as block:
            @block.sync
            def _(sp):
                for u in range(2):
                    sp.sem_inc(d_qk.sems[u], 16 * 8)

                def load(t, u):
                    s_wtlo.room(sp, t * 2 + u)
                    w = (wq, wk)[u]
                    sp.dma_start(wt[:, u, :, :], w[bass.ds(t, 1)].rearrange("a p (k c) -> p (a k) c", c=P)
                                 ).then_inc(d_wt.sems[u], 16)

                def store(t, u):
                    s_rlo.done(sp, (t * 2 + u) * SC + SC - 1)
                    for part in range(2):
                        for odd in range(2):
                            for h in range(2):
                                r0 = (odd * 2 + h) * HALF
                                sp.dma_start(
                                    qk_dram[u, bass.ds(t * 2 + h, 1), part, odd * HALF:(odd + 1) * HALF, :]
                                    .rearrange("a r s -> (a r) s"),
                                    r_pair[r0:r0 + HALF, u, part, :]).then_inc(d_qk.sems[u], 16)
                load(0, 0)
                sp.dma_start(cos_sb[:, :], cos).then_inc(d_tab.sems[0], 16)
                sp.dma_start(sin_sb[:, :], sin).then_inc(d_tab.sems[0], 16)
                load(0, 1)
                with sp.Fori(0, KT - 1) as t:
                    for u in range(2):
                        load(t + 1, u)
                        store(t, u)
                for u in range(2):
                    store(KT - 1, u)
                for u in range(2):
                    d_qk.done(sp, u, KT)

            @block.tensor
            def _(pe):
                s_pq.give(pe)
                with pe.Fori(0, KT) as t:
                    for u in range(2):
                        j = t * 2 + u
                        s_wtlo.done(pe, j)
                        for c in range(SC):
                            s_t1.room(pe, j * SC + c)
                            for k in range(KT):
                                for a, b in ((0, 0), (0, 1), (1, 0)):
                                    mm = pe.matmul(pq[:, c, :], wt_pair[:, u, a, k, :],
                                                   hT[:, b, k, c * CH:(c + 1) * CH],
                                                   start=(k == 0 and a == b), stop=(k == KT - 1 and a == 1))
                            mm.then_inc(s_pq.sem, 1)

            @block.scalar
            def _(a):
                s_rhi.give(a)

                def weights(t, u):
                    d_wt.done(a, u, t)
                    s_pq.room(a, (t * 2 + u) * SC + SC - 1)
                    a.activation(wt_pair[:, u, 0, :, :], wt[:, u, :, :], ACT.Copy,
                                 scale=col(wfac, (Q_, K_)[u])).then_inc(s_wthi.sem, 1)

                def swaps(t, u, c):
                    n = (t * 2 + u) * SC + c
                    s_pq.done(a, n)
                    s_t2.room(a, n)
                    a.activation(swap[0:64, c % 2, :], pq[64:128, c, :], ACT.Copy)
                    a.activation(swap[64:128, c % 2, :], pq[0:64, c, :], ACT.Copy).then_inc(s_sw.sem, 1)

                def hi(t, u, c):
                    s_r.done(a, (t * 2 + u) * SC + c)
                    if c == 0:
                        d_qk.done(a, u, t)
                    a.activation(r_pair[:, u, 0, c * CH:(c + 1) * CH], rot[:, c % 2, 0, :], ACT.Copy,
                                 scale=QKV_DOWN).then_inc(s_rhi.sem, 1)

                def tile(t, u, last):
                    for c in range(SC):
                        swaps(t, u, c)
                        if c == 1 and not last:
                            weights(t + u, 1 - u)
                        hi(t, u, c)

                weights(0, 0)
                with a.Fori(0, KT - 1) as t:
                    tile(t, 0, False)
                    tile(t, 1, False)
                tile(KT - 1, 0, False)
                tile(KT - 1, 1, True)

            @block.vector
            def _(v):
                for s in (s_wtlo, s_t1, s_t2, s_rlo):
                    s.give(v)
                d_tab.done(v, 0, 0)

                def weights(t, u):
                    s_wthi.done(v, t * 2 + u)
                    v.scalar_tensor_tensor(out=wt_pair[:, u, 1, :, :], in0=wt[:, u, :, :],
                                           scalar=col(wfac, (Q_, K_)[u]), in1=wt_pair[:, u, 0, :, :],
                                           op0=ALU.mult, op1=ALU.subtract).then_inc(s_wtlo.sem, 1)

                def tile(t, u, last):
                    for c in range(SC):
                        n = (t * 2 + u) * SC + c
                        tok = slice(c * CH, (c + 1) * CH)
                        s_sw.done(v, n)
                        s_rlo.room(v, n)
                        v.tensor_tensor(rot[:, c % 2, 0, :], pq[:, c, :], cos_sb[:, tok],
                                        ALU.mult).then_inc(s_t1.sem, 1)
                        v.tensor_tensor(rot[:, c % 2, 1, :], swap[:, c % 2, :], sin_sb[:, tok],
                                        ALU.mult).then_inc(s_t2.sem, 1)
                        if c == 1 and not last:
                            weights(t + u, 1 - u)
                        s_t1.done(v, n)
                        s_t2.done(v, n)
                        v.tensor_tensor(rot[:, c % 2, 0, :], rot[:, c % 2, 0, :], rot[:, c % 2, 1, :],
                                        ALU.add).then_inc(s_r.sem, 1)
                        s_rhi.done(v, n)
                        v.scalar_tensor_tensor(out=r_pair[:, u, 1, tok], in0=rot[:, c % 2, 0, :],
                                               scalar=QKV_DOWN, in1=r_pair[:, u, 0, tok], op0=ALU.mult,
                                               op1=ALU.subtract).then_inc(s_rlo.sem, 1)
                weights(0, 0)
                with v.Fori(0, KT - 1) as t:
                    tile(t, 0, False)
                    tile(t, 1, False)
                tile(KT - 1, 0, False)
                tile(KT - 1, 1, True)
        c2.close()


        order = [15, 3, 11, 7, 14, 2, 10, 6, 13, 1, 9, 5, 12, 0, 8, 4]
        tiles = [(u, qt) for u in range(2) for qt in order]
        chunks = [-(-(qt + 1) // SC) for _, qt in tiles]
        first = [sum(chunks[:m]) for m in range(len(tiles))]
        NT, NCH = len(tiles), sum(chunks)
        S_RING, P_RING, T_RING, PT_RING = 5, 8, 2, 4
        assert NCH % S_RING == NCH % P_RING == NCH % T_RING == NCH % PT_RING == 0

        def width(m, c):
            return min(SC, tiles[m][1] + 1 - SC * c)

        place = [(m, c) for m in range(NT) for c in range(chunks[m])]
        LAG_EXP, LAG_T, LAG_PV = 4, 6, 8

        def slots(eng, slot):
            def look(t, z, last):
                def at(lag):
                    g0 = z - lag
                    if g0 < 0 or (last and g0 >= NCH):
                        return None
                    return (t, g0, t * NCH + g0) if g0 < NCH else (t + 1, g0 - NCH, t * NCH + g0)
                return at
            for z in range(LAG_PV):
                slot(look(0, z, False))
            with eng.Fori(0, HEADS // 2 - 1) as t:
                for z in range(LAG_PV, LAG_PV + NCH):
                    slot(look(t, z, False))
            for z in range(LAG_PV, LAG_PV + NCH):
                slot(look(HEADS // 2 - 1, z, True))

        c3 = ctx.enter_context(ExitStack())
        q_sb = sb("q_sb", [P, 2, S], F16, c3)
        k_sb = sb("k_sb", [P, 2, 2, S], F16, c3)
        probs = sb("probs", [P, P_RING, CH], F32, c3)
        pt_pair = sb("pt_pair", [P, PT_RING, 2, CH], F16, c3)
        mx = sb("mx", [P, NT, SC], F32, c3)
        nbias = sb("nbias", [P, NT], F32, c3)
        o_lo = sb("o_lo", [P, 2, D], F32, c3)
        sp_ = ps("logits", [P, S_RING, CH], F32, c3)
        tp3 = ps("tp3", [P, T_RING, CH], F32, c3)
        op_bank = ps("op_bank", [P, CH], F32, c3)
        op = op_bank[:, 0:2 * D]
        d_q = loads("d_q", 2, 5)
        s_QK = signal("s_QK", 2 * (NCH // 2))
        s_mx = signal("s_mx")
        s_cm = signal("s_cm")
        s_nb = signal("s_nb")
        s_P = signal("s_P", S_RING)
        s_PT = signal("s_PT", P_RING)
        s_pthi = signal("s_pthi")
        s_ptlo = signal("s_ptlo", T_RING)
        s_PV = signal("s_PV", PT_RING)
        s_olo = signal("s_olo")
        s_o = signal("s_o", 1)
        with nc.Block() as block:
            @block.sync
            def _(sp):
                with sp.Fori(0, HEADS // 2) as t:
                    for u in range(2):
                        head = t * 2 + u
                        s_QK.room(sp, (head + 1) * (NCH // 2) - 1)
                        sem_u = d_q.sems[u]
                        sp.dma_start(q_sb[:, u, :], qk_dram[0, bass.ds(head, 1)].rearrange("a b r s -> (a b r) s")
                                     ).then_inc(sem_u, 16)
                        for part in range(2):
                            for copy in range(2):
                                sp.dma_start(k_sb[copy * D:(copy + 1) * D, u, part, :],
                                             qk_dram[1, bass.ds(head, 1), part].rearrange("a r s -> (a r) s")
                                             ).then_inc(sem_u, 16)

            @block.gpsimd
            def _(pool):
                with pool.Fori(0, HEADS // 2) as t:
                    for m in range(NT):
                        s_cm.done(pool, t * NT + m)
                        pool.tensor_tensor(nbias[:, m:m + 1], mx[:, m, 0:1], col(coef, 0),
                                           ALU.mult).then_inc(s_nb.sem, 1)

            @block.tensor
            def _(pe):
                for s in (s_QK, s_PT, s_PV):
                    s.give(pe)

                def logits(t, g0, g):
                    m, c = place[g0]
                    (u, qt), w = tiles[m], width(m, c)
                    if m % (NT // 2) == 0 and c == 0:
                        d_q.done(pe, u, t)
                    s_P.room(pe, g)
                    bank = sp_[:, g0 % S_RING, 0:w * P]
                    diagonal = c == chunks[m] - 1
                    for part in range(2):
                        mm = pe.matmul(bank, q_sb[:, u, qt * P:(qt + 1) * P],
                                       k_sb[:, u, part, c * CH:c * CH + w * P],
                                       start=(part == 0), stop=(part == 1 and not diagonal))
                    if diagonal:
                        mm = pe.matmul(sp_[:, g0 % S_RING, (w - 1) * P:w * P], ident_bf[:, :],
                                       mask_bf[:, :], start=False, stop=True)
                    mm.then_inc(s_QK.sem, 1)

                def transposes(t, g0, g):
                    w = width(*place[g0])
                    s_P.done(pe, g)
                    s_ptlo.room(pe, g)
                    for k in range(w):
                        mm = pe.transpose(tp3[:, g0 % T_RING, k * P:(k + 1) * P],
                                          probs[:, g0 % P_RING, k * P:(k + 1) * P], ident[:, :])
                    mm.then_inc(s_PT.sem, 1)

                def times_v(t, g0, g):
                    m, c = place[g0]
                    u, qt = tiles[m]
                    s_ptlo.done(pe, g)
                    if c == 0:
                        s_o.room(pe, t * NT + m)
                    for k in range(width(m, c)):
                        kt = c * SC + k
                        v_at = v_rows[:, kt, bass.ds(t * 2 + u, 1), :].rearrange("p a c -> p (a c)")
                        v_hi_at = v_rows[:, kt, bass.ds(t * 2 + u, 1), 0:D].rearrange("p a c -> p (a c)")
                        at = slice(k * P, (k + 1) * P)
                        pe.matmul(op[:, :], pt_pair[:, g0 % PT_RING, 0, at], v_at,
                                  start=(kt == 0), stop=False)
                        mm = pe.matmul(op[:, 0:D], pt_pair[:, g0 % PT_RING, 1, at], v_hi_at,
                                       start=False, stop=(kt == qt))
                    mm.then_inc(s_PV.sem, 1)

                def slot(at):
                    for lag, stage in ((0, logits), (LAG_T, transposes), (LAG_PV, times_v)):
                        if at(lag):
                            stage(*at(lag))
                slots(pe, slot)

            @block.scalar
            def _(a):
                s_P.give(a)

                def exponentials(t, g0, g):
                    m, c = place[g0]
                    (u, qt), w = tiles[m], width(m, c)
                    if c == 0:
                        s_nb.done(a, t * NT + m)
                    s_PT.room(a, g)
                    a.activation(probs[:, g0 % P_RING, 0:w * P], sp_[:, g0 % S_RING, 0:w * P],
                                 ACT.Exp, bias=nbias[:, m:m + 1], scale=col(coef, 0),
                                 accum_out=sums[:, qt, bass.ds(t * 2 + u, 1), c:c + 1]
                                 .rearrange("p a c -> p (a c)")).then_inc(s_P.sem, 1)

                def hi(t, g0, g):
                    w = width(*place[g0])
                    s_PT.done(a, g)
                    s_PV.room(a, g)
                    a.activation(pt_pair[:, g0 % PT_RING, 0, 0:w * P], tp3[:, g0 % T_RING, 0:w * P],
                                 ACT.Copy, scale=P_SCALE).then_inc(s_pthi.sem, 1)

                def p_v_lo(t, g0, g):
                    m, c = place[g0]
                    if c == chunks[m] - 1:
                        s_PV.done(a, g)
                        s_o.room(a, t * NT + m)
                        a.activation(o_lo[:, m % 2, :], op[:, D:2 * D], ACT.Copy).then_inc(s_olo.sem, 1)

                def slot(at):
                    for lag, stage in ((LAG_EXP, exponentials), (LAG_T, hi), (LAG_PV, p_v_lo)):
                        if at(lag):
                            stage(*at(lag))
                slots(a, slot)

            @block.vector
            def _(v):
                for s in (s_ptlo, s_o):
                    s.give(v)

                def maximum(t, g0, g):
                    m, c = place[g0]
                    s_QK.done(v, g)
                    v.tensor_reduce(mx[:, m, c:c + 1], sp_[:, g0 % S_RING, 0:width(m, c) * P], AX_X, ALU.max,
                                    negate=True).then_inc(s_mx.sem, 1)

                def tile_maximum(t, g0, g):
                    m, c = place[g0]
                    if c == chunks[m] - 1:
                        s_mx.done(v, g)
                        if c:
                            v.tensor_reduce(mx[:, m, 0:1], mx[:, m, 0:c + 1], AX_X,
                                            ALU.min).then_inc(s_cm.sem, 1)
                        else:
                            v.sem_inc(s_cm.sem, 1)

                def lo(t, g0, g):
                    w = width(*place[g0])
                    s_pthi.done(v, g)
                    v.scalar_tensor_tensor(out=pt_pair[:, g0 % PT_RING, 1, 0:w * P],
                                           in0=tp3[:, g0 % T_RING, 0:w * P], scalar=P_SCALE,
                                           in1=pt_pair[:, g0 % PT_RING, 0, 0:w * P], op0=ALU.mult,
                                           op1=ALU.subtract).then_inc(s_ptlo.sem, 1)

                def output(t, g0, g):
                    m, c = place[g0]
                    u, qt = tiles[m]
                    if c == chunks[m] - 1:
                        s_olo.done(v, t * NT + m)
                        o_at = o_rows[:, qt, bass.ds((t * 2 + u) * D, D)]
                        v.tensor_tensor(o_at, op[:, 0:D], o_lo[:, m % 2, :], ALU.add).then_inc(s_o.sem, 1)

                def slot(at):
                    for lag, stage in ((0, maximum), (LAG_PV, output), (0, tile_maximum), (LAG_T, lo)):
                        if at(lag):
                            stage(*at(lag))
                slots(v, slot)
        c3.close()

        c4 = ctx.enter_context(ExitStack())
        wo_pair = sb("wo_pair", [P, 2, KT, E], F16, c4)
        xres = sb("xres", [P, 2, E], F32, c4)
        on = sb("on", [P, E], F32, c4)
        oT = sb("oT", [P, 2, 2, KT, P], F16, c4)
        at = sb("at", [P, 2, E], F32, c4)
        xn = sb("xn", [P, 2, E], F32, c4)
        rinv = sb("rinv", [P, ST, HEADS], F32, c4)
        st4 = sb("st4", [P, 2, 36], F32, c4)
        tp4 = ps("tp4", [P, KT, P], F32, c4)
        ap4 = ps("ap4", [P, 2, 2, CH], F32, c4)
        tp5 = ps("tp5", [P, KT, P], F32, c4)
        d_wo = loads("d_wo", 2)
        d_xr = loads("d_xr", 2)
        d_x1 = loads("d_x1", 2)
        s_c4 = sem("s_c4")
        s_wohi = signal("s_wohi")
        s_wolo = signal("s_wolo", 2)
        s_on = signal("s_on")
        s_t4 = signal("s_t4", 1)
        s_ohi = signal("s_ohi")
        s_ol4 = signal("s_ol4", 1)
        s_mm = signal("s_mm", 2)
        s_rs = signal("s_rs")
        s_ap = signal("s_ap", 2)
        s_x1 = signal("s_x1", 2)
        s_raw4 = signal("s_raw4")
        s_var4 = signal("s_var4")
        s_eps4 = signal("s_eps4")
        s_root4 = signal("s_root4")
        s_var5 = signal("s_var5")
        s_eps5 = signal("s_eps5")
        s_root5 = signal("s_root5")
        s_xn = signal("s_xn", 2)
        s_t5 = signal("s_t5", 2)
        s_xhi = signal("s_xhi")
        s_xlo = signal("s_xlo", 1)
        CHAIN4 = 8

        def scaled_variance(v, st, n, variance):
            v.tensor_scalar(st[:, 13:14], st[:, 13:14], col(coef, n), col(coef, n), ALU.mult, ALU.mult
                            ).then_inc(variance.sem, 1)

        def norm_scale(v, chain, st, n):
            chain.link(v.tensor_scalar(st[:, 14:15], st[:, 14:15], col(coef, n), None, ALU.mult))
            chain.wait()
            return v.tensor_scalar(st[:, 15:16], st[:, 12:13], st[:, 14:15], -1.0, ALU.mult, ALU.mult)

        with nc.Block() as block:
            @block.sync
            def _(sp):
                wo_v = wo.rearrange("(k p) n -> p k n", p=P)
                for u in range(2):
                    sp.sem_inc(d_x1.sems[u], 16)
                for k in range(KT):
                    s_wolo.room(sp, k)
                    sp.dma_start(xres[:, k % 2, :], wo_v[:, k, :]).then_inc(d_wo.sems[k % 2], 16)
                s_wolo.done(sp, KT - 1)

                def load(st):
                    i, u = st.item(1), st.slot(1)
                    d_x1.done(sp, u, st.use(1))
                    s_xn.room(sp, i)
                    sp.dma_start(xres[:, u, :], x_tiles[bass.ds(i, 1)].rearrange("a p e -> p (a e)")
                                 ).then_inc(d_xr.sems[u], 16)

                def step(st):
                    if st.has(-1, ST):
                        i, u = st.item(-1), st.slot(-1)
                        s_x1.done(sp, i)
                        sp.dma_start(x1_dram[bass.ds(i * P, P), :], xres[:, u, :]).then_inc(d_x1.sems[u], 16)
                    if st.has(1, ST):
                        load(st)
                pipeline(sp, step, 2, 2, ST)
                for u in range(2):
                    d_x1.done(sp, u, ST // 2)

            @block.gpsimd
            def _(pool):
                with pool.Fori(0, ST // 2) as it:
                    for u in range(2):
                        s_var4.done(pool, it * 2 + u)
                        inverse_root(pool, st4[:, u, 0:16], s_eps4, s_root4, it * 2 + u)
                        s_var5.done(pool, it * 2 + u)
                        inverse_root(pool, st4[:, u, 16:36], s_eps5, s_root5, it * 2 + u)

            @block.tensor
            def _(pe):
                for s in (s_t4, s_mm, s_t5):
                    s.give(pe)
                s_wolo.done(pe, KT - 1)

                def step(st):
                    if st.has(1, ST):
                        i = st.item(1)
                        s_on.done(pe, i)
                        s_ol4.room(pe, i)
                        for k in range(KT):
                            mm = pe.transpose(tp4[:, k, :], on[:, k * P:(k + 1) * P], ident[:, :])
                        mm.then_inc(s_t4.sem, 1)
                    if st.has(0, ST):
                        i, u = st.item(0), st.slot(0)
                        s_ol4.done(pe, i)
                        s_ap.room(pe, i)
                        for n in range(2):
                            for k in range(KT):
                                for a, b in ((0, 0), (0, 1), (1, 0)):
                                    mm = pe.matmul(ap4[:, u, n, :], oT[:, u, a, k, :],
                                                   wo_pair[:, b, k, n * CH:(n + 1) * CH],
                                                   start=(k == 0 and a == b), stop=(k == KT - 1 and a == 1))
                        mm.then_inc(s_mm.sem, 1)
                    if st.has(-1, ST):
                        i, u = st.item(-1), st.slot(-1)
                        s_xn.done(pe, i)
                        s_xlo.room(pe, i)
                        for k in range(KT):
                            mm = pe.transpose(tp5[:, k, :], xn[:, u, k * P:(k + 1) * P], ident[:, :])
                        mm.then_inc(s_t5.sem, 1)
                pipeline(pe, step, 2, 2, ST)

            @block.scalar
            def _(a):
                s_ap.give(a)
                for k in range(KT):
                    d_wo.done(a, k % 2, k // 2)
                    a.activation(wo_pair[:, 0, k, :], xres[:, k % 2, :], ACT.Copy,
                                 scale=col(wfac, O_)).then_inc(s_wohi.sem, 1)

                def step(st):
                    if st.has(-2, ST):
                        i = st.item(-2)
                        s_t5.done(a, i)
                        a.activation(xnT[:, 0, :, bass.ds(i * P, P)], tp5[:, :, :], ACT.Copy
                                     ).then_inc(s_xhi.sem, 1)
                    if st.has(1, ST):
                        i, u = st.item(1), st.slot(1)
                        s_t4.done(a, i)
                        s_mm.room(a, i)
                        a.activation(oT[:, u, 0, :, :], tp4[:, :, :], ACT.Copy).then_inc(s_ohi.sem, 1)
                    if st.has(-1, ST):
                        i, u = st.item(-1), st.slot(-1)
                        s_rs.done(a, i)
                        s_x1.room(a, i)
                        a.activation(at[:, u, :], ap4[:, u, :, :].rearrange("p n c -> p (n c)"), ACT.Identity,
                                     bias=st4[:, u, 15:16], scale=st4[:, u, 14:15]).then_inc(s_ap.sem, 1)
                pipeline(a, step, 2, 2, ST)

            @block.vector
            def _(v):
                for s in (s_wolo, s_ol4, s_x1, s_xn, s_xlo):
                    s.give(v)
                chain = Chain(v, s_c4)
                chain.link(v.tensor_reduce(rinv[:, :, :], sums[:, :, :, :], AX_X, ALU.add))
                chain.wait()
                chain.link(v.reciprocal(rinv[:, :, :], rinv[:, :, :]))
                chain.wait()
                chain.link(v.tensor_scalar(rinv[:, :, :], rinv[:, :, :], 1.0 / P_SCALE, None, ALU.mult))
                for k in range(KT):
                    s_wohi.done(v, k)
                    v.scalar_tensor_tensor(out=wo_pair[:, 1, k, :], in0=xres[:, k % 2, :], scalar=col(wfac, O_),
                                           in1=wo_pair[:, 0, k, :], op0=ALU.mult,
                                           op1=ALU.subtract).then_inc(s_wolo.sem, 1)
                chain.wait()
                start = chain.at

                def step(st):
                    if st.has(-2, ST):
                        i = st.item(-2)
                        s_xhi.done(v, i)
                        v.tensor_tensor(xnT[:, 1, :, bass.ds(i * P, P)], tp5[:, :, :],
                                        xnT[:, 0, :, bass.ds(i * P, P)], ALU.subtract).then_inc(s_xlo.sem, 1)
                    if st.has(1, ST):
                        i, u = st.item(1), st.slot(1)
                        s_ohi.done(v, i)
                        v.tensor_tensor(oT[:, u, 1, :, :], tp4[:, :, :], oT[:, u, 0, :, :],
                                        ALU.subtract).then_inc(s_ol4.sem, 1)
                    if st.has(2, ST):
                        i = st.item(2)
                        s_t4.room(v, i)
                        v.tensor_tensor(on[:, :].rearrange("p (h d) -> p h d", d=D),
                                        o_rows[:, bass.ds(i, 1), :].rearrange("p a (h d) -> p (a h) d", d=D),
                                        rinv[:, bass.ds(i, 1), :].rearrange("p a h -> p (a h)").unsqueeze(2)
                                        .to_broadcast([P, HEADS, D]), ALU.mult).then_inc(s_on.sem, 1)
                    if st.has(-1, ST):
                        i, u = st.item(-1), st.slot(-1)
                        chain = Chain(v, s_c4, i * CHAIN4 + start)
                        s1, s2 = st4[:, u, 0:16], st4[:, u, 16:36]
                        s_mm.done(v, i)
                        layernorm_stats(v, chain, (ap4[:, u, 0, :], ap4[:, u, 1, :]), s1, s_raw4)
                        s_raw4.done(v, i)
                        scaled_variance(v, s1, 1, s_var4)
                        s_root4.done(v, i)
                        norm_scale(v, chain, s1, 1).then_inc(s_rs.sem, 1)
                        d_xr.done(v, u, st.use(-1))
                        s_ap.done(v, i)
                        v.tensor_tensor(xres[:, u, :], xres[:, u, :], at[:, u, :], ALU.add).then_inc(s_x1.sem, 1)
                        s_x1.done(v, i)
                        layernorm_stats(v, chain, (xres[:, u, 0:CH], xres[:, u, CH:E]), s2, s_var5)
                        s_root5.done(v, i)
                        chain.link(v.tensor_scalar(s2[:, 14:15], s2[:, 14:15], H_SCALE, None, ALU.mult))
                        chain.wait()
                        s_t5.room(v, i)
                        v.tensor_scalar(xn[:, u, :], xres[:, u, :], s2[:, 12:13], s2[:, 14:15], ALU.subtract,
                                        ALU.mult).then_inc(s_xn.sem, 1)
                pipeline(v, step, 2, 2, ST)
        c4.close()
        c04.close()

        c5 = ctx.enter_context(ExitStack())
        wgu = sb("wgu", [P, 2, 2, 2, KT * GW], F16, c5)
        wd = sb("wd", [P, 2, 2 * E], F16, c5)
        inter = sb("inter", [P, 2, 2, 2, CH], F16, c5)
        sg = sb("sg", [P, 2, CH], F32, c5)
        cst = sb("cst", [P, 2, CH], I32, c5)
        sst = sb("sst", [P, 2, CH], F32, c5)
        code7 = sb("code7", [P, CH], F32, c5)
        line = sb("line", [P, 4, CH], F32, c5)
        below = sb("below", [P, 2, CH], F32, c5)
        above = sb("above", [P, CH], F32, c5)
        gp = ps("gp", [P, 2, 2, CH], F32, c5)
        yp = ps("yp", [P, 4, CH], F32, c5)
        offsets = sb("offsets", [P, 9], F32, c5)
        d_st = loads("d_st", 2, 3)
        s_off = signal("s_off")
        s_c7 = signal("s_c7", 2)
        s_L = signal("s_L", 1)
        s_use = signal("s_use", 6)
        s_nf = signal("s_nf")
        s_w = signal("s_w", 2)
        s_whi = signal("s_whi")
        s_wlo = signal("s_wlo")
        s_g = signal("s_g")
        s_u = signal("s_u", 1)
        s_sg = signal("s_sg")
        s_it = signal("s_it", 2)
        s_ihi = signal("s_ihi")
        s_ilo = signal("s_ilo", 2)
        s_y = signal("s_y", 16)
        s_add = signal("s_add", 4)
        s_z = signal("s_z")
        late = wgu[:, NG % 2, :, :, :].rearrange("p m a c -> p (m a c)").bitcast(F32).rearrange(
            "p (b u e) -> p b u e", b=2, u=2)
        x1t, yn = late[:, 0], late[:, 1]
        st6 = sb("st6", [P, 2, 16], F32, c5)
        d_x1l = loads("d_x1l", 2)
        d_out = loads("d_out", 2)
        s_c6 = sem("s_c6")
        s_raw6 = signal("s_raw6")
        s_var6 = signal("s_var6")
        s_eps6 = signal("s_eps6")
        s_root6 = signal("s_root6")
        s_rs6 = signal("s_rs6")
        s_yn = signal("s_yn", 2)
        s_out = signal("s_out", 2)
        CHAIN6 = 4
        out_tiles = out.rearrange("(t p) e -> t p e", p=P)
        x1_tiles = x1_dram.rearrange("(t p) e -> t p e", p=P)
        LEAD = 2 * UNITS
        PER = 3 * UNITS
        EVS = 2 * SC
        ADDS = 8 * SC
        LINE_ROOM = [-2, -2, -1, 0, 1, 1, 2, 3]

        def group_events(last):
            ev = []
            r = e = 0
            for c in range(SC):
                for _ in range(2):
                    ev += [("DQ", r), ("EV", e)]
                    r, e = r + 1, e + 1
                if c:
                    ev.append(("ADD", c - 1, r))
                    r += 1
            ev.append(("ADD", SC - 1, r))
            if last:
                ev = [("ADD", x[1], None) if x[0] == "ADD" and x[2] >= UNITS else x for x in ev
                      if not (x[0] == "DQ" and x[1] >= UNITS)]
            return ev

        def unit_place(r, par):
            m, q = divmod(r, UNITS)
            cols = slice(q * CH, (q + 1) * CH)
            if m == 0:
                return 2, wd[:, 0, cols], wd[:, 1, cols], q
            return m - 1, wgu[:, 1 - par, m - 1, 0, cols], wgu[:, 1 - par, m - 1, 1, cols], q

        def groups(eng, body):
            with eng.Fori(0, (NG - 1) // 2) as it:
                for par in range(2):
                    body(it * 2 + par, par, False)
            body(NG - 1, (NG - 1) % 2, True)
        assert NG % 2 == 1 and LEAD % 2 == 0 and PER % 2 == 0

        with nc.Block() as block:
            @block.sync
            def _(sp):
                def load(n, slot, m, g, q):
                    s_c7.room(sp, n)
                    s_w.room(sp, n)
                    cols = slice(q * CH, (q + 1) * CH)
                    sp.dma_start(cst[:, slot, :], codes[m][bass.ds(g, 1), :, cols].rearrange("a p c -> p (a c)")
                                 ).then_inc(d_st.sems[slot], 16)
                    for half in range(2):
                        sp.dma_start(sst[half * BLOCK:(half + 1) * BLOCK, slot, :],
                                     scales[m][bass.ds(g, 1), half, cols].to_broadcast([BLOCK, CH])
                                     ).then_inc(d_st.sems[slot], 16)

                for n in range(LEAD):
                    load(n, n % 2, n // UNITS, 0, n % UNITS)

                def body(g, par, last):
                    for r in range(UNITS if last else PER):
                        m, _, _, q = unit_place(r, par)
                        load(g * PER + (LEAD + r), r % 2, m, g if r < UNITS else g + 1, q)
                groups(sp, body)

                for u in range(2):
                    sp.sem_inc(d_out.sems[u], 16)
                s_u.done(sp, (NG - 1) * EVS - 1)

                def rows(st):
                    if st.has(1, ST):
                        i, u = st.item(1), st.slot(1)
                        d_out.done(sp, u, st.use(1))
                        sp.dma_start(x1t[:, u, :], x1_tiles[bass.ds(i, 1)].rearrange("a p e -> p (a e)")
                                     ).then_inc(d_x1l.sems[u], 16)
                    if st.has(0, ST):
                        i, u = st.item(0), st.slot(0)
                        s_out.done(sp, i)
                        sp.dma_start(out_tiles[bass.ds(i, 1)].rearrange("a p e -> p (a e)"), x1t[:, u, :]
                                     ).then_inc(d_out.sems[u], 16)
                pipeline(sp, rows, 2, 2, ST)
                for u in range(2):
                    d_out.done(sp, u, ST // 2)

            @block.gpsimd
            def _(pool):
                pool.memset(y_rows[:, :, :], 0.0).then_inc(s_z.sem, 1)
                with pool.Fori(0, ST // 2) as it:
                    for u in range(2):
                        s_var6.done(pool, it * 2 + u)
                        inverse_root(pool, st6[:, u, :], s_eps6, s_root6, it * 2 + u)

            @block.tensor
            def _(pe):
                s_u.give(pe)
                s_y.give(pe)

                def body(g, par, last):
                    def gate_up(c):
                        tok = slice(c * CH, (c + 1) * CH)
                        for t in range(2):
                            e = c * 2 + t
                            s_it.room(pe, g * EVS + e)
                            for m, s in ((0, s_g), (1, s_u)):
                                for k in range(KT):
                                    col0 = k * GW + t * P
                                    for a, b in ((0, 0), (0, 1), (1, 0)):
                                        mm = pe.matmul(gp[:, e % 2, m, :], wgu[:, par, m, a, col0:col0 + P],
                                                       xnT[:, b, k, tok], start=(k == 0 and a == b),
                                                       stop=(k == KT - 1 and a == 1))
                                mm.then_inc(s.sem, 1)

                    def down(c):
                        s_ilo.done(pe, g * EVS + (c * 2 + 1))
                        for j in range(SC):
                            for n in range(2):
                                d = c * 8 + j * 2 + n
                                s_add.room(pe, g * ADDS + d)
                                for t in range(2):
                                    for a, b in ((0, 0), (0, 1), (1, 0)):
                                        mm = pe.matmul(yp[:, d % 4, :], inter[:, c % 2, a, t, j * P:(j + 1) * P],
                                                       wd[:, b, t * E + n * CH:t * E + (n + 1) * CH],
                                                       start=(t == 0 and a == b), stop=(t == 1 and a == 1))
                                mm.then_inc(s_y.sem, 1)

                    s_wlo.done(pe, g * PER + (LEAD - 1))
                    gate_up(0)
                    for c in range(1, SC):
                        gate_up(c)
                        if c == 1:
                            s_wlo.done(pe, g * PER + (LEAD + UNITS - 1))
                        down(c - 1)
                    down(SC - 1)
                groups(pe, body)

            @block.scalar
            def _(a):
                s_c7.give(a)
                s_L.give(a)
                s_off.done(a, 0)
                pending = []

                def flush():
                    while pending:
                        pending.pop(0)()

                def dequantise(n, slot, use, m, hi_out, free):
                    d_st.done(a, slot, use)
                    s_L.done(a, n * 8 + (-1))
                    a.activation(code7[:, :], cst[:, slot, :], ACT.Identity, bias=offsets[:, 8:9]
                                 ).then_inc(s_c7.sem, 1)
                    s_c7.done(a, n)
                    for k, (slope, _) in enumerate(BELOW + ABOVE):
                        if k == 4:
                            flush()
                        a.wait_ge(s_use.sem, n * 6 + (6 + LINE_ROOM[k]))
                        a.activation(line[:, k % 4, :], code7[:, :], ACT.Identity, scale=slope,
                                     bias=offsets[:, k:k + 1]).then_inc(s_L.sem, 1)

                    def hi():
                        s_w.done(a, n)
                        free()
                        a.activation(hi_out, below[:, slot, :], ACT.Copy, scale=col(wfac, G_ + m)
                                     ).then_inc(s_whi.sem, 1)
                    pending.append(hi)

                for n in range(LEAD):
                    m, q = divmod(n, UNITS)
                    dequantise(n, n % 2, n // 2, m, wgu[:, 0, m, 0, q * CH:(q + 1) * CH], lambda: None)

                def body(g, par, last):
                    for ev in group_events(last):
                        r = ev[2] if ev[0] == "ADD" else ev[1] if ev[0] == "DQ" else None
                        if r is not None:
                            m, hi_out, _, _ = unit_place(r, par)
                            free = ((lambda: s_y.done(a, g * ADDS + (-1))) if r < UNITS
                                    else (lambda: s_u.done(a, g * EVS + (-1))))
                            dequantise(g * PER + (LEAD + r), r % 2, g * (PER // 2) + ((LEAD + r) // 2), m,
                                       hi_out, free)
                        if ev[0] == "EV":
                            e = ev[1]
                            s_g.done(a, g * EVS + e)
                            s_ilo.room(a, g * EVS + e)
                            a.activation(sg[:, e % 2, :], gp[:, e % 2, 0, :], ACT.Silu, scale=col(coef, 2)
                                         ).then_inc(s_sg.sem, 1)
                            flush()

                            def hi(e=e):
                                s_it.done(a, g * EVS + e)
                                s_y.room(a, g * ADDS + (e // 2 * 8 + 7))
                                a.activation(inter[:, e // 2 % 2, 0, e % 2, :], sg[:, e % 2, :], ACT.Copy
                                             ).then_inc(s_ihi.sem, 1)
                            pending.append(hi)
                        if r is None and ev[0] == "ADD":
                            flush()
                        if last and ev[0] == "ADD":
                            for i in range(ev[1] * SC, (ev[1] + 1) * SC):
                                norm_rows(i)
                    flush()

                def norm_rows(i):
                    u = i % 2
                    s_rs6.done(a, i)
                    s_out.room(a, i)
                    a.activation(yn[:, u, :], y_rows[:, i, :], ACT.Identity, bias=st6[:, u, 15:16],
                                 scale=st6[:, u, 14:15]).then_inc(s_yn.sem, 1)
                s_yn.give(a)
                flush()
                groups(a, body)

            @block.vector
            def _(v):
                for s in (s_use, s_w, s_it, s_ilo, s_add, s_out):
                    s.give(v)
                for k, (_, offset) in enumerate(BELOW + ABOVE):
                    v.memset(offsets[:, k:k + 1], offset)
                v.memset(offsets[:, 8:9], -float(ZERO_CODE)).then_inc(s_off.sem, 1)
                pending = []

                def flush():
                    while pending:
                        pending.pop(0)()

                def dequantise(n, slot, m, lo_out, hi_out, beside=()):
                    beside = list(beside)
                    b = below[:, slot, :]

                    def first(out, k, op):
                        s_L.done(v, n * 8 + (k + 1))
                        v.scalar_tensor_tensor(out=out, in0=line[:, k % 4, :], scalar=0.0,
                                               in1=line[:, (k + 1) % 4, :], op0=op, op1=op).then_inc(s_use.sem, 1)

                    def more(out, k, op):
                        s_L.done(v, n * 8 + k)
                        v.wait_ge(s_use.sem, n * 6 + (6 + {2: 1, 3: 2, 6: 4, 7: 5}[k]))
                        v.tensor_tensor(out, out, line[:, k % 4, :], op).then_inc(s_use.sem, 1)

                    def total():
                        v.wait_ge(s_use.sem, n * 6 + 12)
                        v.tensor_tensor(b, b, above[:, :], ALU.add).then_inc(s_nf.sem, 1)

                    def scale():
                        s_nf.done(v, n)
                        v.tensor_tensor(b, b, sst[:, slot, :], ALU.mult).then_inc(s_w.sem, 1)

                    ops = [lambda: first(b, 0, ALU.min), lambda: more(b, 2, ALU.min), lambda: more(b, 3, ALU.min),
                           lambda: first(above[:, :], 4, ALU.max), lambda: more(above[:, :], 6, ALU.max),
                           lambda: more(above[:, :], 7, ALU.max), total, scale]
                    for k, op in enumerate(ops):
                        op()
                        if k == 0:
                            flush()
                        if beside:
                            beside.pop(0)()

                    def lo():
                        s_whi.done(v, n)
                        v.scalar_tensor_tensor(out=lo_out, in0=b, scalar=col(wfac, G_ + m), in1=hi_out,
                                               op0=ALU.mult, op1=ALU.subtract).then_inc(s_wlo.sem, 1)
                    pending.append(lo)

                for n in range(LEAD):
                    m, q = divmod(n, UNITS)
                    cols = slice(q * CH, (q + 1) * CH)
                    dequantise(n, n % 2, m, wgu[:, 0, m, 1, cols], wgu[:, 0, m, 0, cols])
                flush()

                def body(g, par, last):
                    def add(c, k):
                        d = c * 8 + k
                        j, n = divmod(k, 2)
                        y_at = y_rows[:, c * SC + j, n * CH:(n + 1) * CH]
                        s_y.done(v, g * ADDS + d)
                        s_add.room(v, g * ADDS + d)
                        v.tensor_tensor(y_at, yp[:, d % 4, :], y_at, ALU.add).then_inc(s_add.sem, 1)

                    for ev in group_events(last):
                        r = ev[2] if ev[0] == "ADD" else ev[1] if ev[0] == "DQ" else None
                        adds = [lambda k=k, c=ev[1]: add(c, k) for k in range(8)] if ev[0] == "ADD" else []
                        if r is not None:
                            m, hi_out, lo_out, _ = unit_place(r, par)
                            dequantise(g * PER + (LEAD + r), r % 2, m, lo_out, hi_out, adds)
                        elif adds:
                            flush()
                            for k, f in enumerate(adds):
                                f()
                                if k % 2:
                                    i = ev[1] * SC + k // 2
                                    if i % SC:
                                        factors(i - 1)
                                    statistics(i)
                                    outputs(i - 2)
                            factors(i)
                            outputs(i - 1)
                        if ev[0] == "EV":
                            e = ev[1]
                            s_sg.done(v, g * EVS + e)
                            s_u.done(v, g * EVS + e)
                            v.scalar_tensor_tensor(out=sg[:, e % 2, :], in0=gp[:, e % 2, 1, :],
                                                   scalar=col(coef, 3), in1=sg[:, e % 2, :], op0=ALU.mult,
                                                   op1=ALU.mult).then_inc(s_it.sem, 1)
                            flush()

                            def lo(e=e):
                                s_ihi.done(v, g * EVS + e)
                                v.tensor_tensor(inter[:, e // 2 % 2, 1, e % 2, :], sg[:, e % 2, :],
                                                inter[:, e // 2 % 2, 0, e % 2, :], ALU.subtract
                                                ).then_inc(s_ilo.sem, 1)
                            pending.append(lo)
                    if last:
                        outputs(ST - 1)
                    flush()

                def statistics(i):
                    u = i % 2
                    chain = Chain(v, s_c6, i * CHAIN6)
                    s_yn.room(v, i)
                    s_add.done(v, (NG - 1) * ADDS + (i * 2 + 1))
                    layernorm_stats(v, chain, (y_rows[:, i, 0:CH], y_rows[:, i, CH:E]), st6[:, u, :], s_raw6)
                    s_raw6.done(v, i)
                    scaled_variance(v, st6[:, u, :], 4, s_var6)

                def factors(i):
                    chain = Chain(v, s_c6, i * CHAIN6 + CHAIN6 - 1)
                    s_root6.done(v, i)
                    norm_scale(v, chain, st6[:, i % 2, :], 4).then_inc(s_rs6.sem, 1)

                s_z.done(v, 0)

                stored = []

                def outputs(until):
                    while len(stored) <= until:
                        i = len(stored)
                        stored.append(i)
                        d_x1l.done(v, i % 2, i // 2)
                        s_yn.done(v, i)
                        v.tensor_tensor(x1t[:, i % 2, :], x1t[:, i % 2, :], yn[:, i % 2, :], ALU.add
                                        ).then_inc(s_out.sem, 1)
                groups(v, body)
        c5.close()


def kernel(**inputs):
    import concourse.bacc as bacc
    from concourse.bass_utils import run_bass_kernel_spmd

    x = np.ascontiguousarray(inputs["L0_attn_hidden_states"]).reshape(S, E)

    order = [h * D + 2 * i + odd for t in range(KT) for odd in range(2) for h in (2 * t, 2 * t + 1)
             for i in range(HALF)]

    def tiled(w):
        w = np.ascontiguousarray(w)[:, order].reshape(KT, P, KT, P)
        return np.ascontiguousarray(w.transpose(2, 1, 0, 3)).reshape(KT, P, E)

    inv_freq = (1.0 / np.float32(10000.0) ** (np.arange(0, D, 2, dtype=np.float32) / np.float32(D))
                ).astype(np.float32)
    angle = np.arange(S, dtype=np.float32)[:, None] * inv_freq[None, :]
    cos = np.ascontiguousarray(np.tile(np.cos(angle.astype(np.float64)).astype(np.float32).T, (4, 1)))
    sin = np.ascontiguousarray(np.tile(np.sin(angle.astype(np.float64)).astype(np.float32).T, (4, 1)))

    def padded(a, axis, n):
        widths = [(0, 0), (0, 0)]
        widths[axis] = (0, n - a.shape[axis])
        return np.pad(np.ascontiguousarray(a), widths)

    arrays = {"x": x, "wq": tiled(inputs["L0_attn_Wq"]), "wk": tiled(inputs["L0_attn_Wk"]),
              "wv": np.ascontiguousarray(inputs["L0_attn_Wv"]), "wo": np.ascontiguousarray(inputs["L0_attn_Wo"]),
              "cos": cos, "sin": sin}
    for name in ("gate", "up"):
        c = padded(inputs[f"L0_ffn_{name}_codes"], 0, IP).T.reshape(KT, P, NG, GW)
        arrays[f"{name}_codes"] = np.ascontiguousarray(c.transpose(2, 1, 0, 3)).reshape(NG, P, KT * GW)
        s = padded(inputs[f"L0_ffn_{name}_scales"], 0, IP).T.reshape(KT, 2, NG, GW)
        arrays[f"{name}_scales"] = np.ascontiguousarray(s.transpose(2, 1, 0, 3)).reshape(NG, 2, KT * GW)
    c = padded(inputs["L0_ffn_down_codes"], 1, IP).T.reshape(NG, 2, P, E)
    arrays["down_codes"] = np.ascontiguousarray(c.transpose(0, 2, 1, 3)).reshape(NG, P, 2 * E)
    s = padded(inputs["L0_ffn_down_scales"], 1, IP // BLOCK).T.reshape(NG, 2, 2, E)
    arrays["down_scales"] = np.ascontiguousarray(s.transpose(0, 2, 1, 3)).reshape(NG, 2, 2 * E)
    for name in ("gate", "up", "down"):
        flat = np.ascontiguousarray(inputs[f"L0_ffn_{name}_scales"])
        arrays[f"{name}_flat"] = flat.reshape(P, I * E // BLOCK // P)

    nc = bacc.Bacc("TRN2", target_bir_lowering=False, num_devices=1)
    t = {k: nc.dram_tensor(f"in_{k}", a.shape, mybir.dt.from_np(a.dtype), kind="ExternalInput").ap()
         for k, a in arrays.items()}
    out = nc.dram_tensor("out_0", (S, E), F32, kind="ExternalOutput").ap()
    names = ("gate", "up", "down")
    build(nc, t["x"], t["wq"], t["wk"], t["wv"], t["wo"], t["cos"], t["sin"],
          [t[f"{n}_codes"] for n in names], [t[f"{n}_scales"] for n in names],
          [t[f"{n}_flat"] for n in names], out)
    r = run_bass_kernel_spmd(nc, [{f"in_{k}": a for k, a in arrays.items()}], core_ids=[0])
    return r.results[0]["out_0"].reshape(1, S, E)
```
